# Optimizing a Trainium2 kernel written in Bass

```python
import numpy as np
import jax
import jax.numpy as jnp

def _softmax(x, axis=-1):
    return jax.nn.softmax(x, axis=axis)

def _gelu(x):
    return jax.nn.gelu(x, approximate=True)

def _silu(x):
    return jax.nn.silu(x)

def _sigmoid(x):
    return jax.nn.sigmoid(x)

def _layernorm(x, axis=-1, eps=1e-05):
    m = jnp.mean(x, axis=axis, keepdims=True)
    v = jnp.var(x, axis=axis, keepdims=True)
    return (x - m) / jnp.sqrt(v + eps)

def _scatter_add(tgt, idx, src, axis=0):
    return tgt.at[idx].add(src)

def _segment_sum(src, seg, n):
    return jax.ops.segment_sum(src, seg, n)
kernel_name = 'mk_gnn_resnorm_d4_gnn_r16_9fa0d0'

def setup_inputs(seed: int=0):
    np.random.seed(seed)
    _w = jnp.asarray

    def _rec_inputs():
        import jax
        import jax.numpy as jnp
        _gk = jax.random.key(seed)
        x = -0.0005121 + 1.001 * jax.random.normal(jax.random.fold_in(_gk, 1), (6250, 64), jnp.float32)
        _s = jax.random.randint(jax.random.fold_in(_gk, 2), (100000,), 0, 6250, jnp.int32)
        _d = jax.random.randint(jax.random.fold_in(_gk, 3), (100000,), 0, 6250, jnp.int32)
        _loop = jnp.arange(6250, dtype=jnp.int32)
        src = jnp.concatenate([_s, _d, _loop])
        dst = jnp.concatenate([_d, _s, _loop])
        _o = jnp.argsort(dst, stable=True)
        src = src[_o]
        dst = dst[_o]
        edge_attr_64 = 0.000189758 + 1.00013 * jax.random.normal(jax.random.fold_in(_gk, 12), (206250, 64), jnp.float32)
        return (x, src, dst, edge_attr_64)
    x, src, dst, edge_attr_64 = _rec_inputs()

    def _L0_gnn_setup():
        import jax, jax.numpy as jnp
        import numpy as np
        N_NODES = 3125
        N_EDGES = 50000
        IN_F = 64
        OUT_F = 64
        BN_EPS = 1e-05
        key = jax.random.key(seed)
        k1, k2, k3 = jax.random.split(key, 3)
        x = jax.random.normal(k1, (N_NODES, IN_F), dtype=jnp.float32)
        edge_index = jax.random.randint(k2, (2, N_EDGES), 0, N_NODES, dtype=jnp.int64)
        W = jax.random.normal(k3, (IN_F, OUT_F), dtype=jnp.float32) * (1.0 / np.sqrt(IN_F))
        b = jnp.zeros((OUT_F,), dtype=jnp.float32)
        gamma = jnp.ones((OUT_F,), dtype=jnp.float32)
        beta = jnp.zeros((OUT_F,), dtype=jnp.float32)
        return {'x': x, 'edge_index': edge_index, 'W': W, 'b': b, 'gamma': gamma, 'beta': beta}
    _L0_gnn_all = _L0_gnn_setup()
    _L0_gnn_in = {k: v for k, v in _L0_gnn_all.items() if k in ('W', 'b', 'gamma', 'beta')}
    del _L0_gnn_all

    def _L1_gnn_setup():
        import jax, jax.numpy as jnp
        import numpy as np
        N, E, D, H = (6250, 50000, 64, 4)
        O = D

        def _ln(x, g, b, eps=1e-05):
            m = x.mean(-1, keepdims=True)
            v = ((x - m) ** 2).mean(-1, keepdims=True)
            return (x - m) * jax.lax.rsqrt(v + eps) * g + b

        def _leaky(x):
            return jnp.where(x >= 0, x, 0.01 * x)
        key = jax.random.key(seed)
        ks = jax.random.split(key, 12)

        def xavier(k, shape):
            lim = np.sqrt(6.0 / (shape[-2] + shape[-1]))
            return jax.random.uniform(k, shape, jnp.float32, -lim, lim)
        return {'x': jax.random.normal(ks[0], (N, D), jnp.float32), 'edge_index': jax.random.randint(ks[1], (2, E), 0, N, jnp.int32), 'edge_feature': jax.random.normal(ks[2], (E, D), jnp.float32), 'Kv2v': xavier(ks[3], (H, D, O)), 'Ke2v': xavier(ks[4], (H, D, O)), 'Vv2v': xavier(ks[5], (H, D, O)), 'Ve2v': xavier(ks[6], (H, D, O)), 'Wu': xavier(ks[7], (H, 2 * O, 2 * O)), 'bu': jnp.zeros((H, 2 * O), jnp.float32), 'ln_g': jnp.ones((H, 2 * O), jnp.float32), 'ln_b': jnp.zeros((H, 2 * O), jnp.float32), 'Wm': xavier(ks[8], (H, 2 * O, O)), 'bm': jnp.zeros((H, O), jnp.float32), 'mln_g': jnp.ones((H, O), jnp.float32), 'mln_b': jnp.zeros((H, O), jnp.float32), 'Wc': xavier(ks[9], (H * O, O)), 'bc': jnp.zeros((O,), jnp.float32), 'bn_g': jnp.ones((O,), jnp.float32), 'bn_b': jnp.zeros((O,), jnp.float32)}
    _L1_gnn_all = _L1_gnn_setup()
    _L1_gnn_in = {k: v for k, v in _L1_gnn_all.items() if k in ('Kv2v', 'Ke2v', 'Vv2v', 'Ve2v', 'Wu', 'bu', 'ln_g', 'ln_b', 'Wm', 'bm', 'mln_g', 'mln_b', 'Wc', 'bc', 'bn_g', 'bn_b')}
    del _L1_gnn_all

    def _L2_gnn_setup():
        import jax, jax.numpy as jnp
        import numpy as np
        N_NODES = 3125
        N_EDGES = 50000
        D_FEAT = 64
        key = jax.random.key(seed)
        k_x, k_e, k_w = jax.random.split(key, 3)
        x = jax.random.normal(k_x, (N_NODES, D_FEAT), dtype=jnp.float32)
        edge_index = jax.random.randint(k_e, (2, N_EDGES), 0, N_NODES, dtype=jnp.int64)
        W = jax.random.normal(k_w, (D_FEAT, D_FEAT), dtype=jnp.float32) / np.sqrt(D_FEAT)
        b = jnp.zeros((D_FEAT,), dtype=jnp.float32)
        return {'x': x, 'edge_index': edge_index, 'W': W, 'b': b}
    _L2_gnn_all = _L2_gnn_setup()
    _L2_gnn_in = {k: v for k, v in _L2_gnn_all.items() if k in ('W', 'b')}
    del _L2_gnn_all

    def _L3_gnn_setup():
        import jax, jax.numpy as jnp
        import numpy as np
        EPS = 1e-12

        def _l2_normalize(x):
            n = jnp.linalg.norm(x, axis=-1, keepdims=True)
            return x / jnp.maximum(n, EPS)
        key = jax.random.key(seed)
        k1, k2, k3 = jax.random.split(key, 3)
        N, E, D = (6250, 75000, 64)
        feat = jax.random.normal(k1, (N, D), dtype=jnp.float32)
        beta = jnp.ones((1,), dtype=jnp.float32)
        src = jax.random.randint(k2, (E,), 0, N, dtype=jnp.int32)
        dst = jax.random.randint(k3, (E,), 0, N, dtype=jnp.int32)
        return {'feat': feat, 'beta': beta, 'src': src, 'dst': dst}
    _L3_gnn_all = _L3_gnn_setup()
    _L3_gnn_in = {k: v for k, v in _L3_gnn_all.items() if k in ('beta',)}
    del _L3_gnn_all
    return {'x': x, 'src': src, 'dst': dst, 'edge_attr_64': edge_attr_64, 'L0_gnn_W': _L0_gnn_in['W'], 'L0_gnn_b': _L0_gnn_in['b'], 'L0_gnn_gamma': _L0_gnn_in['gamma'], 'L0_gnn_beta': _L0_gnn_in['beta'], 'L1_gnn_Kv2v': _L1_gnn_in['Kv2v'], 'L1_gnn_Ke2v': _L1_gnn_in['Ke2v'], 'L1_gnn_Vv2v': _L1_gnn_in['Vv2v'], 'L1_gnn_Ve2v': _L1_gnn_in['Ve2v'], 'L1_gnn_Wu': _L1_gnn_in['Wu'], 'L1_gnn_bu': _L1_gnn_in['bu'], 'L1_gnn_ln_g': _L1_gnn_in['ln_g'], 'L1_gnn_ln_b': _L1_gnn_in['ln_b'], 'L1_gnn_Wm': _L1_gnn_in['Wm'], 'L1_gnn_bm': _L1_gnn_in['bm'], 'L1_gnn_mln_g': _L1_gnn_in['mln_g'], 'L1_gnn_mln_b': _L1_gnn_in['mln_b'], 'L1_gnn_Wc': _L1_gnn_in['Wc'], 'L1_gnn_bc': _L1_gnn_in['bc'], 'L1_gnn_bn_g': _L1_gnn_in['bn_g'], 'L1_gnn_bn_b': _L1_gnn_in['bn_b'], 'L2_gnn_W': _L2_gnn_in['W'], 'L2_gnn_b': _L2_gnn_in['b'], 'L3_gnn_beta': _L3_gnn_in['beta']}

def reference(x, src, dst, edge_attr_64, L0_gnn_W, L0_gnn_b, L0_gnn_gamma, L0_gnn_beta, L1_gnn_Kv2v, L1_gnn_Ke2v, L1_gnn_Vv2v, L1_gnn_Ve2v, L1_gnn_Wu, L1_gnn_bu, L1_gnn_ln_g, L1_gnn_ln_b, L1_gnn_Wm, L1_gnn_bm, L1_gnn_mln_g, L1_gnn_mln_b, L1_gnn_Wc, L1_gnn_bc, L1_gnn_bn_g, L1_gnn_bn_b, L2_gnn_W, L2_gnn_b, L3_gnn_beta):
    import jax
    import jax.numpy as jnp

    def _L0_gnn_ref(x, edge_index, W, b, gamma, beta):
        import jax, jax.numpy as jnp
        import numpy as np
        N_NODES = 3125
        N_EDGES = 50000
        IN_F = 64
        OUT_F = 64
        BN_EPS = 1e-05
        N = x.shape[0]
        loop = jnp.arange(N, dtype=edge_index.dtype)
        src = jnp.concatenate([edge_index[0], loop])
        dst = jnp.concatenate([edge_index[1], loop])
        deg = jnp.zeros((N,), dtype=x.dtype).at[dst].add(1.0)
        dinv = jnp.where(deg > 0, jax.lax.rsqrt(deg), 0.0)
        norm = dinv[src] * dinv[dst]
        h = x @ W
        msg = h[src] * norm[:, None]
        out = jax.ops.segment_sum(msg, dst, num_segments=N) + b
        mean = jnp.mean(out, axis=0)
        var = jnp.mean((out - mean) ** 2, axis=0)
        out = (out - mean) * jax.lax.rsqrt(var + BN_EPS) * gamma + beta
        return jax.nn.relu(out)

    def _L1_gnn_ref(x, edge_index, edge_feature, Kv2v, Ke2v, Vv2v, Ve2v, Wu, bu, ln_g, ln_b, Wm, bm, mln_g, mln_b, Wc, bc, bn_g, bn_b):
        import jax, jax.numpy as jnp
        import numpy as np
        N, E, D, H = (6250, 50000, 64, 4)
        O = D

        def _ln(x, g, b, eps=1e-05):
            m = x.mean(-1, keepdims=True)
            v = ((x - m) ** 2).mean(-1, keepdims=True)
            return (x - m) * jax.lax.rsqrt(v + eps) * g + b

        def _leaky(x):
            return jnp.where(x >= 0, x, 0.01 * x)
        src, dst = (edge_index[0], edge_index[1])
        n = x.shape[0]
        scale = 1.0 / np.sqrt(2.0 * O).astype(np.float32)
        heads = []
        for h in range(Kv2v.shape[0]):
            K_v = x @ Kv2v[h]
            V_v = x @ Vv2v[h]
            K_E = edge_feature @ Ke2v[h]
            V_E = edge_feature @ Ve2v[h]
            q_i = K_v[dst]
            alpha = jnp.concatenate([q_i * K_v[src], q_i * K_E], axis=1) * scale
            gate = jax.nn.sigmoid(_ln(alpha, ln_g[h], ln_b[h]))
            m = jnp.concatenate([V_v[src], V_E], axis=1)
            m = (m @ Wu[h] + bu[h]) * gate
            m = _leaky(_ln(m @ Wm[h] + bm[h], mln_g[h], mln_b[h]))
            heads.append(jax.ops.segment_sum(m, dst, num_segments=n))
        hv = jnp.concatenate(heads, axis=1)
        out = hv @ Wc + bc
        mu = out.mean(0)
        var = ((out - mu) ** 2).mean(0)
        out = (out - mu) * jax.lax.rsqrt(var + 1e-05) * bn_g + bn_b
        return _leaky(out) + x

    def _L2_gnn_ref(x, edge_index, W, b):
        import jax, jax.numpy as jnp
        import numpy as np
        N_NODES = 3125
        N_EDGES = 50000
        D_FEAT = 64
        src = edge_index[0]
        dst = edge_index[1]
        n_nodes = x.shape[0]
        x_j = x[src]
        msg = jax.nn.relu(jnp.einsum('ed,df->ef', x_j, W) + b)
        out = jax.ops.segment_sum(msg, dst, num_segments=n_nodes)
        return out

    def _L3_gnn_ref(feat, beta, src, dst):
        import jax, jax.numpy as jnp
        import numpy as np
        EPS = 1e-12

        def _l2_normalize(x):
            n = jnp.linalg.norm(x, axis=-1, keepdims=True)
            return x / jnp.maximum(n, EPS)
        N = feat.shape[0]
        nh = _l2_normalize(feat)
        e = beta[0] * jnp.sum(nh[src] * nh[dst], axis=-1)
        emax = jax.ops.segment_max(e, dst, num_segments=N)
        emax = jnp.where(jnp.isfinite(emax), emax, 0.0)
        p = jnp.exp(e - emax[dst])
        psum = jax.ops.segment_sum(p, dst, num_segments=N)
        p = p / jnp.maximum(psum[dst], EPS)
        msg = feat[src] * p[:, None]
        out = jax.ops.segment_sum(msg, dst, num_segments=N)
        return out
    edge_index = jnp.stack([src, dst])
    x = _layernorm(x + _L0_gnn_ref(x, edge_index, L0_gnn_W, L0_gnn_b, L0_gnn_gamma, L0_gnn_beta), axis=-1)
    x = _layernorm(x + _L1_gnn_ref(x, edge_index, edge_attr_64, L1_gnn_Kv2v, L1_gnn_Ke2v, L1_gnn_Vv2v, L1_gnn_Ve2v, L1_gnn_Wu, L1_gnn_bu, L1_gnn_ln_g, L1_gnn_ln_b, L1_gnn_Wm, L1_gnn_bm, L1_gnn_mln_g, L1_gnn_mln_b, L1_gnn_Wc, L1_gnn_bc, L1_gnn_bn_g, L1_gnn_bn_b), axis=-1)
    x = _layernorm(x + _L2_gnn_ref(x, edge_index, L2_gnn_W, L2_gnn_b), axis=-1)
    x = _layernorm(x + _L3_gnn_ref(x, L3_gnn_beta, src, dst), axis=-1)
    return x

_drawn_inputs = setup_inputs


def setup_inputs(seed=0):
    import zlib

    import numpy as np

    out = dict(_drawn_inputs(seed))
    spreads = {'L0_gnn_b': (0.0, 0.8),
     'L0_gnn_gamma': (1.0, 0.2),
     'L0_gnn_beta': (0.0, 0.1),
     'L1_gnn_bu': (0.0, 0.311),
     'L1_gnn_ln_g': (1.0, 0.6),
     'L1_gnn_ln_b': (0.0, 0.737),
     'L1_gnn_bm': (0.0, 0.1),
     'L1_gnn_mln_g': (1.0, 0.2),
     'L1_gnn_mln_b': (0.0, 0.342),
     'L1_gnn_bc': (0.0, 0.8),
     'L1_gnn_bn_g': (1.0, 0.2),
     'L1_gnn_bn_b': (0.0, 0.1),
     'L2_gnn_b': (0.0, 0.1)}
    factors = {}
    for name, (base, spread) in spreads.items():
        noise = np.random.default_rng([zlib.crc32(name.encode()), seed]).standard_normal(out[name].shape)
        drawn = base * np.exp(spread * noise) if base else spread * noise
        out[name] = jnp.asarray(drawn.astype(out[name].dtype))
    for name, factor in factors.items():
        out[name] = (out[name] * factor).astype(out[name].dtype)
    return out
```

```python
from contextlib import ExitStack

import concourse.bass as bass
from concourse import mybir

F32 = mybir.dt.float32
BF16 = mybir.dt.bfloat16
I32 = mybir.dt.int32
ALU = mybir.AluOpType
ACT = mybir.ActivationFunctionType
AX = mybir.AxisListType.X
DVE = mybir.EngineType.DVE
PE = mybir.EngineType.PE

P = 128
N = 6250
E = 206250
D = 64
H = 4
G = 4
U = 4
T = -(-E // (P * U * G)) * U * G
NG = T // G
NC = -(-N // P)
NP = NC * P
WIN = P
NW = NP + WIN
LO = 64
HI = NP // LO
HG = 8
NB = 7
BC = NC // NB
ROW1 = D + H * D
ROW3 = D + 2
SUM3 = D + 1
EPS = 1e-5
EPS1 = 128 * EPS
EPS_NORM = 1e-12
NBLK = -(-NP // 512)
TC = [min(P, T - i) for i in range(0, T, P)]
BIG = 1.0e30
MAGIC = float(0x5F3759DF)
assert NC == NB * BC and HI * LO == NP and T % (2 * HG) == 0


def steps(eng, body, n, first, last=0, u=U):
    for g in range(first):
        body(g, g // u, g % u, False)
    with eng.Fori(first // u, n // u) as k:
        for s in range(u):
            body(u * k + s, k, s, True)
    for g in range(n, n + last):
        body(g, g // u, g % u, False)


def after(eng, semaphore, value):
    if not isinstance(value, int) or value > 0:
        eng.wait_ge(semaphore, value)


def gnn(nc, a, out):
    ctx = ExitStack()
    with ctx:
        def sb(name, shape, dt=F32):
            return ctx.enter_context(nc.sbuf_tensor(name, shape, dt))

        def sem(name):
            return ctx.enter_context(nc.semaphore(name))

        def dram(name, shape, dt=F32):
            return nc.dram_tensor(name, shape, dt, kind="Internal").ap()

        table0 = dram("table0", (NP, D))
        table1 = dram("table1", (NP, ROW1))
        table1q = dram("table1q", (NP, H * D))
        table2 = dram("table2", (NP, D))
        table3 = dram("table3", (NP, ROW3))
        kept_rows = dram("kept_rows", (NG, P, G * ROW3))
        dinv_flat = dram("dinv_flat", (NP,))
        score_lin = dram("score_lin", (T * P,))
        shift_lin = dram("shift_lin", (T * P,))
        edge_ids = dram("edge_ids", (2 * P,))
        edge_max = dram("edge_max", (2 * P,))

        acc = sb("acc", [P, 2, NW])
        src_t = sb("src_t", [P, T], I32)
        dst_t = sb("dst_t", [P, T], I32)
        rel = sb("rel", [P, T])
        xn = sb("xn", [P, NC, D])
        iota_i = sb("iota_i", [P, P], I32)
        iota_f = sb("iota_f", [P, P])
        part_i = sb("part_i", [P, 1], I32)
        part_f = sb("part_f", [P, 1])
        ident = sb("ident", [P, P])
        idx_src = [sb(f"idx_src{s}", [P, G], I32) for s in range(U)]
        idx_dst = [sb(f"idx_dst{s}", [P, G], I32) for s in range(2)]
        w0 = sb("w0", [D, D])
        w2 = sb("w2", [D, D])
        kv = sb("kv", [D, H * D])
        ke = sb("ke", [P, H * D])
        v_blocks = sb("v_blocks", [P, H, P])
        wu = sb("wu", [P, H, P])
        wvu = sb("wvu", [P, H, P])
        wm = sb("wm", [P, H, D])
        wc = sb("wc", [P, 2, D])
        cols = sb("cols", [P, 3, H])
        vecs = sb("vecs", [D, 6])
        bm_row = sb("bm_row", [1, H, D])
        bm_rest = sb("bm_rest", [1, H, D])
        bm_up = sb("bm_up", [1, H, D])
        bm_part = [sb(f"bm_part{i}", [1, H * D], BF16) for i in range(3)]
        bm_parts = sb("bm_parts", [3, H * D], BF16)
        ones3 = sb("ones3", [3, P], BF16)
        mg = sb("mg", [P, H * D])
        mb = sb("mb", [P, H * D])
        b2 = sb("b2", [P, D])
        beta3 = sb("beta3", [P, 1])
        small = sb("small", [P, 64])
        dn = sb("dn", [P, NC])

        arena = sb("arena", [P, 25600])
        top = [0]

        def view(words, shape, parts=(0, P), dt=F32):
            at = arena[parts[0]:parts[1], top[0]:top[0] + words]
            top[0] += words
            at = at if dt == F32 else at.bitcast(dt)
            if len(shape) > 1:
                names = "abcde"[:len(shape)]
                at = at.rearrange(f"p ({' '.join(names)}) -> p {' '.join(names)}",
                                  **dict(zip(names, shape)))
            return at

        top[0] = 0
        fm = view(NP, [NP], (0, D))
        xa = view(NC * D, [NC, D])
        xb = view(NC * D, [NC, D])
        stage = [view(BC * ROW1, [BC, ROW1]) for _ in range(2)]
        bn_out = view(13 * 6, [13, 6])
        assert top[0] <= 25600
        fm_c = fm.rearrange("f (p c) -> f c p", c=NC)
        hist_sb = xa.rearrange("p c d -> p (c d)")[0:HI, 0:2 * LO].rearrange("p (a b) -> p a b", a=2)
        tab3 = view(NC * ROW3, [NC, ROW3])
        top[0] = 0
        hi_i, lo_i = view(T, [T], dt=I32), view(T, [T], dt=I32)
        hi_f, lo_f = view(T, [T]), view(T, [T])
        base_b = view(T, [T], dt=I32)
        one_hi = [view(HG * HI // 2, [HG, HI], dt=BF16) for _ in range(2)]
        one_lo = [view(HG * LO // 2, [HG, LO], dt=BF16) for _ in range(2)]
        top[0] = 0
        onehot = [view(G * WIN, [G, WIN]) for _ in range(2)]
        rows = [view(G * D, [G, D]) for _ in range(U)]
        rows3 = [view(G * ROW3, [G, ROW3]) for _ in range(U)]
        xs_t = [view(G * P, [G, P], (0, D)) for _ in range(2)]
        picked = [view(G * WIN, [G, WIN]) for _ in range(2)]
        e_raw = [view(G, [G]) for _ in range(2)]
        score = view(T, [T])
        turned = view(len(TC) * P, [len(TC), P])
        lin = view(T, [T])
        dst_lin = view(T, [T], dt=I32)
        dst_lf = view(T, [T])
        pen = view(T + 1, [T + 1])
        fwd = view(T, [T])
        seg = view(T, [T])
        eq = view(T, [T])
        ends = view(8, [8])
        ids_b = view(2 * P, [2 * P])
        max_b = view(2 * P, [2 * P])
        scr_b = view(2 * P, [2 * P])
        assert top[0] <= 25600
        top[0] = 2 * G * WIN
        xk = [view(G * ROW1, [G, ROW1]) for _ in range(2)]
        q = [view(G * H * D, [G, H, D]) for _ in range(2)]
        xt = [view(G * P, [G, P]) for _ in range(2)]
        alpha = [view(G * H * P, [G, H, 2, D]) for _ in range(2)]
        gate = [view(H * G * P, [H, G * P]) for _ in range(2)]
        gm = view(H * G * P, [H, G, P])
        o_sb = [view(G * H * D, [G * H, D]) for _ in range(2)]
        o_sq = [view(G * H * D, [G * H, D]) for _ in range(2)]
        y = view(G * H * D, [G * H, D])
        msg = [view(G * H * D, [G * H, D]) for _ in range(2)]
        st = view(G * H * 6, [G * H, 6])
        tmp = [view(2 * G * H, [2 * G * H]) for _ in range(5)]
        rstd = view(2 * G * H, [2 * G * H])
        shift = view(G * H, [G * H])
        assert top[0] <= 25600, top[0]

        psum = ctx.enter_context(nc.psum_tensor("psum", [P, 8, 512], F32))
        node_ps = [psum[:, 4 * r:4 * r + 4, :].rearrange("p b n -> p (b n)") for r in range(2)]

        nh_t = acc[0:D, 1, :]
        nh_c = acc[0:D, 1, 0:NP].rearrange("f (p c) -> f c p", c=NC)
        acc_c = acc[:, 0, 0:NP].rearrange("f (p c) -> f c p", c=NC)
        dinv_cols = acc[0:D, 1, 0:NP]

        s_load = sem("s_load")
        s_vload = sem("s_vload")
        s_iota = sem("s_iota")
        dve_step = sem("dve_step")
        act_step = sem("act_step")
        pe_batch = sem("pe_batch")
        hot_ready = sem("hot_ready")
        hist_done = sem("hist_done")
        dinv_out = sem("dinv_out")
        dinv_in = sem("dinv_in")
        bm_in = sem("bm_in")
        t0_out = sem("t0_out")
        t1_out = [sem(f"t1_out{r}") for r in range(2)]
        t2_out = sem("t2_out")
        t3_out = sem("t3_out")
        score_out = sem("score_out")
        score_in = sem("score_in")
        ends_out = sem("ends_out")
        ends_in = sem("ends_in")
        shift_out = sem("shift_out")
        shift_in = sem("shift_in")
        out_done = sem("out_done")
        gather_go = sem("gather_go")
        turn_go = sem("turn_go")

        class Plain:

            def __init__(self, tag):
                self.idx = sem(f"idx_ready{tag}")
                self.rows_in = [sem(f"rows_in{tag}_{s}") for s in range(U)]
                self.hot = sem(f"onehot_ready{tag}")
                self.sums = sem(f"sums_done{tag}")
                self.added = sem(f"added{tag}")

        p0, p2 = Plain("0"), Plain("2")
        a_idx = sem("idx_ready3a")
        a_in = [sem(f"rows_in3a_{s}") for s in range(U)]
        a_turned = sem("turned3a")
        a_xt = sem("xs_t_ready3a")
        a_dots = sem("dots_done3a")
        a_hot = sem("onehot_ready3a")
        a_pick = sem("picked3a")
        a_red = sem("reduced3a")
        a_score = sem("scores3a")
        a_kept = [sem(f"kept3a_{s}") for s in range(U)]
        b_in = [sem(f"rows_in3b_{s}") for s in range(U)]
        b_hot = sem("weights_ready3b")
        b_sums = sem("sums_done3b")
        b_added = sem("added3b")

        idx_ready = sem("idx_ready1")
        kv_in = [sem(f"kv_in{s}") for s in range(2)]
        q_in = [sem(f"q_in{s}") for s in range(2)]
        ea_in = [sem(f"ea_in{s}") for s in range(2)]
        ke_done = sem("ke_done")
        alpha_v = sem("alpha_v")
        alpha_e = sem("alpha_e")
        stats1 = sem("stats1")
        chain1 = sem("chain1")
        normed = sem("normed")
        alpha_t = sem("alpha_t")
        gated = sem("gated")
        xt_turned = sem("xt_turned")
        xt_ready = sem("xt_ready")
        m_done = sem("m_done")
        gm_ready = sem("gm_ready")
        o_done = sem("o_done")
        o_taken = sem("o_taken")
        chain2 = sem("chain2")
        sums1 = sem("sums1")
        added1 = sem("added1")
        CH = 19
        C2 = 5

        block = ctx.enter_context(nc.Block())

        loads = [
            (dst_t[:, :], a["dst_t"]),
            (base_b, a["dst_t"][0:1, :].to_broadcast([P, T])),
            (src_t[:, :], a["src_t"]),
            (xn[:, :, :], a["x"].rearrange("(p c) d -> p c d", c=NC)),
            (w0[:, :], a["w0"]), (w2[:, :], a["w2"]), (kv[:, :], a["kv"]),
            (ke[D:P, :], a["ke"]), (wu[:, :, :], a["wu"]), (wm[:, :, :], a["wm"]),
            (wc[:, :, :], a["wc"]), (cols[:, :, :], a["cols"]), (vecs[:, :], a["vecs"]),
            (bm_row[:, :, :], a["bm"]), (mg[:, :], a["mg"].to_broadcast([P, H * D])),
            (mb[:, :], a["mb"].to_broadcast([P, H * D])), (b2[:, :], a["b2"].to_broadcast([P, D])),
            (beta3[:, :], a["beta3"].to_broadcast([P, 1])),
        ]
        ALL_IN = 16 * len(loads)

        marks, vcount = {}, [0]
        act_order = ["deg", "bn0", "relu0", "ln0"] + [f"fm{i}" for i in range(NBLK)] + \
                    ["bn1", "ln1", "ln2", "nrm", "exp", "ln3"]
        act_number = {name: i + 1 for i, name in enumerate(act_order)}
        pe_number, at = {}, 0
        for name, count in [("fuse", 1), ("table0", NB), ("self0", NBLK), ("y0_n", NB), ("x1_f", NB), ("table1", NB),
                            ("wc", NBLK), ("y1_n", NB), ("x2_f", NB), ("table2", NB), ("y2_n", NB),
                            ("nh_f", NB), ("turn_out", len(TC)), ("turn_in", len(TC)), ("y3_n", NB)]:
            for b in range(count):
                at += 1
                pe_number[name, b] = at

        def bases(engine, tiles):
            _, regs = nc.values_load_multi_w_load_instructions(
                tiles, engines=(engine,), min_val=0, max_val=N,
                skip_runtime_bounds_check_because="destinations are nodes")
            return regs

        def tile_bases(engine, g):
            return bases(engine, dst_t[0:1, bass.ds(g * G, G)])

        @block.vector
        def _(dve):
            V = nc.vector

            def link(ins, mark=None):
                vcount[0] += 1
                ins.then_inc(dve_step, 1)
                dve.wait_ge(dve_step, vcount[0])
                if mark:
                    marks[mark] = vcount[0]

            def act_done(name):
                dve.wait_ge(act_step, act_number[name])

            def wide(v):
                return v.unsqueeze(2).to_broadcast([P, NC, D])

            def rows_norm(dst, src, spare, name):
                total, mean = small[:, 0:NC], dn[:, :]
                link(V.tensor_reduce(total, src, AX, ALU.add))
                link(V.tensor_scalar(mean, total, 1.0 / D, None, ALU.mult))
                link(V.tensor_tensor(src, src, wide(mean), ALU.subtract))
                link(V.tensor_tensor(spare, src, src, ALU.mult))
                link(V.tensor_reduce(total, spare, AX, ALU.add))
                link(V.tensor_scalar(total, total, 1.0 / D, EPS, ALU.mult, ALU.add), mark=name)
                act_done(name)
                link(V.reciprocal(mean, total))
                link(V.tensor_tensor(dst, src, wide(mean), ALU.mult), mark=name + "_out")

            def bn_vectors(name, gamma, beta, src):
                sizes = [(i, min(512, N - i)) for i in range(0, N, 512)]
                for j, (i, n) in enumerate(sizes):
                    link(V.bn_stats(bn_out[0:D, j, :], src[:, i:i + n]))
                mean, var = small[0:D, 50:51], small[0:D, 51:52]
                scale, shift_ = small[0:D, 54:55], small[0:D, 56:57]
                link(V.bn_aggr(small[0:D, 50:52], bn_out[0:D, 0:len(sizes), :].rearrange("p a b -> p (a b)")))
                link(V.tensor_scalar(var, var, EPS, None, ALU.add), mark=name)
                act_done(name)
                link(V.reciprocal(small[0:D, 53:54], var))
                link(V.tensor_tensor(scale, small[0:D, 53:54], gamma, ALU.mult))
                link(V.tensor_tensor(small[0:D, 55:56], scale, mean, ALU.mult))
                link(V.tensor_tensor(shift_, beta, small[0:D, 55:56], ALU.subtract), mark=name + "_vec")
                return scale, shift_

            def evict(name, *ops):
                for b in range(NB):
                    dve.wait_ge(pe_batch, pe_number[name, b])
                    for op in ops:
                        link(op(slice(b * BC, (b + 1) * BC), node_ps[b % 2]), mark=f"{name}{b}")

            def spaced(ps, n):
                return ps[:, 0:BC * P].rearrange("p (c d) -> p c d", c=BC)[:, :, 0:n]

            def one_hot(dst, g):
                return V.tensor_tensor(
                    dst, rel[:, bass.ds(g * G, G)].unsqueeze(2).to_broadcast([P, G, WIN]),
                    iota_f[:, :].unsqueeze(1).to_broadcast([P, G, WIN]), ALU.is_equal)

            def add_tile(added, g, t, at_, sums):
                after(dve, added, g * G + t)
                V.tensor_tensor(at_, at_, sums, ALU.add).then_inc(added, 1)

            link(V.memset(v_blocks[:, :, :], 0.0), mark="v_zero")
            link(V.memset(ones3[:, :], 1.0))
            dve.wait_ge(s_iota, 2)
            link(V.tensor_copy(iota_f[:, :], iota_i[:, :]))
            link(V.tensor_copy(part_f[:, :], part_i[:, :]))
            link(V.tensor_scalar(ident[:, :], iota_f[:, :], part_f[:, 0:1], None, ALU.is_equal))
            dve.wait_ge(s_load, ALL_IN)
            link(V.tensor_tensor(rel[:, :], dst_t[:, :], base_b, ALU.subtract))
            link(V.tensor_scalar(hi_i, dst_t[:, :], 6, None, ALU.arith_shift_right))
            link(V.tensor_scalar(lo_i, dst_t[:, :], LO - 1, None, ALU.bitwise_and))
            link(V.tensor_copy(hi_f, hi_i))
            link(V.tensor_copy(lo_f, lo_i))

            def hist(g, k, s, inside):
                after(dve, hist_done, g - 1)
                V.tensor_tensor(one_hi[s], hi_f[:, bass.ds(g * HG, HG)].unsqueeze(2).to_broadcast([P, HG, HI]),
                                iota_f[:, 0:HI].unsqueeze(1).to_broadcast([P, HG, HI]),
                                ALU.is_equal).then_inc(hot_ready, 1)
                V.tensor_tensor(one_lo[s], lo_f[:, bass.ds(g * HG, HG)].unsqueeze(2).to_broadcast([P, HG, LO]),
                                iota_f[:, 0:LO].unsqueeze(1).to_broadcast([P, HG, LO]),
                                ALU.is_equal).then_inc(hot_ready, 1)
            steps(dve, hist, T // HG, 2, u=2)
            dve.wait_ge(hist_done, T // HG)
            link(V.tensor_scalar(hist_sb[:, 0, :], psum[0:HI, 0, 0:LO], 1.0, None, ALU.add), mark="deg")
            act_done("deg")
            link(V.reciprocal(hist_sb[:, 1, :], hist_sb[:, 0, :]), mark="dinv")

            dve.wait_ge(pe_batch, pe_number["fuse", 0])
            link(V.tensor_copy(wvu[:, :, :], psum[:, 1, :].rearrange("p (h n) -> p h n", h=H)), mark="fused")
            link(V.tensor_reduce(small[:, 0:H], wm[:, :, :], AX, ALU.add))
            link(V.tensor_scalar(small[:, 0:H], small[:, 0:H], 1.0 / D, None, ALU.mult))
            link(V.tensor_tensor(wm[:, :, :], wm[:, :, :],
                                 small[:, 0:H].unsqueeze(2).to_broadcast([P, H, D]), ALU.subtract))
            link(V.tensor_reduce(small[0:1, 0:H], bm_row[:, :, :], AX, ALU.add))
            link(V.tensor_scalar(small[0:1, 0:H], small[0:1, 0:H], 1.0 / D, None, ALU.mult))
            link(V.tensor_tensor(bm_rest[:, :, :], bm_row[:, :, :],
                                 small[0:1, 0:H].unsqueeze(2).to_broadcast([1, H, D]), ALU.subtract))
            for i in range(3):
                part = bm_part[i][:, :].rearrange("p (h d) -> p h d", h=H)
                link(V.tensor_copy(part, bm_rest[:, :, :]), mark="bm_parts")
                if i < 2:
                    link(V.tensor_copy(bm_up[:, :, :], part))
                    link(V.tensor_tensor(bm_rest[:, :, :], bm_rest[:, :, :], bm_up[:, :, :], ALU.subtract))

            dve.wait_ge(dinv_in, 16 * 3)
            evict("table0", lambda c, ps: V.tensor_tensor(
                xa[:, c, :], ps[:, 0:BC * D].rearrange("p (c d) -> p c d", c=BC),
                dn[:, c].unsqueeze(2).to_broadcast([P, BC, D]), ALU.mult))
            for i in range(NBLK):
                dve.wait_ge(pe_batch, pe_number["self0", i])
                n = min(512, NP - 512 * i)
                link(V.tensor_tensor(acc[0:D, 0, 512 * i:512 * i + n], psum[0:D, i % 4, 0:n],
                                     dinv_cols[:, 512 * i:512 * i + n], ALU.mult), mark=f"self0{i}")
            link(V.memset(acc[0:D, 0, NP:NW], 0.0), mark="t0")
            dve.wait_ge(t0_out, 16)

            def plain(p):
                def body(g, k, s, inside):
                    after(dve, p.sums, g - 1)
                    one_hot(onehot[s % 2], g).then_inc(p.hot, 1)
                    if inside or g >= 1:
                        add(g - 1, (s + 1) % 2)

                def add(g, s):
                    regs = tile_bases(DVE, g)
                    dve.wait_ge(p.sums, g + 1)
                    for t in range(G):
                        add_tile(p.added, g, t, acc[0:D, 0, bass.ds(regs[t], WIN)],
                                 psum[0:D, s, t * WIN:(t + 1) * WIN])
                steps(dve, body, NG, U)
                add(NG - 1, 1)
                dve.wait_ge(p.added, T)
            plain(p0)

            link(V.tensor_tensor(fm, acc[0:D, 0, 0:NP], dinv_cols, ALU.mult))
            link(V.tensor_scalar(fm, fm, vecs[:, 0:1], None, ALU.add))
            bn_vectors("bn0", vecs[:, 1:2], vecs[:, 2:3], fm)
            evict("y0_n", lambda c, ps: V.tensor_tensor(xa[:, c, :], spaced(ps, D), xn[:, c, :], ALU.add))
            rows_norm(xn[:, :, :], xa, xb, "ln0")

            evict("x1_f", lambda c, ps: V.tensor_copy(fm_c[:, c, :], spaced(ps[0:D], P)))
            for b in range(NB):
                dve.wait_ge(pe_batch, pe_number["table1", b])
                after(dve, t1_out[b % 2], 32 * (b // 2))
                link(V.tensor_copy(stage[b % 2][:, :, D:ROW1],
                                   node_ps[b % 2][:, 0:BC * H * D].rearrange("p (c n) -> p c n", c=BC)))
                link(V.tensor_copy(stage[b % 2][:, :, 0:D], xn[:, b * BC:(b + 1) * BC, :]), mark=f"table1{b}")
            link(V.memset(acc[:, :, :], 0.0))
            dve.wait_ge(t1_out[0], 32 * 4)
            dve.wait_ge(t1_out[1], 32 * 3)
            for s in range(2):
                link(V.memset(o_sq[s], 1.0), mark="sweep1")

            Q = G * H

            def sweep1(i, k, s, inside):
                now = [inside or 0 <= i - lag < NG for lag in range(4)]
                z = 1 - s
                if now[3]:
                    regs = tile_bases(DVE, i - 3)
                if now[0]:
                    after(dve, alpha_t, H * (i - 1))
                    dve.wait_ge(kv_in[s], 64 * (k + 1))
                    dve.wait_ge(q_in[s], 64 * (k + 1))
                    V.tensor_tensor(alpha[s][:, :, :, 0, :],
                                    xk[s][:, :, D:ROW1].rearrange("p t (h d) -> p t h d", h=H),
                                    q[s], ALU.mult).then_inc(alpha_v, 1)
                    for j in range(2):
                        dve.wait_ge(ke_done, 2 * i + j + 1)
                        V.tensor_tensor(alpha[s][:, 2 * j:2 * j + 2, :, 1, :],
                                        psum[:, 1, :].rearrange("p (t h d) -> p t h d", t=2, h=H),
                                        q[s][:, 2 * j:2 * j + 2, :, :], ALU.mult).then_inc(alpha_e, 1)
                        dve.wait_ge(alpha_v, i + 1)
                        dve.wait_ge(alpha_e, 2 * i + j + 1)
                        for n in range(2 * j * H, 2 * (j + 1) * H):
                            V.bn_stats(st[:, n, :], alpha[s][:, n // H, n % H, :, :].rearrange("p a d -> p (a d)")
                                       ).then_inc(stats1, 1)
                if now[1]:
                    after(dve, o_done, 2 * (i - 1))
                    for h in range(H):
                        dve.wait_ge(m_done, H * (i - 1) + h + 1)
                        dve.wait_ge(gated, H * (i - 1) + h + 1)
                        V.scalar_tensor_tensor(gm[:, h, :, :].rearrange("p t n -> p (t n)"),
                                               psum[:, 4 + h % 2, :], cols[:, 0, h:h + 1],
                                               gate[z][:, h, :], ALU.add, ALU.mult).then_inc(gm_ready, 1)

                n = [0]

                def small_step(ins):
                    ins.then_inc(chain1, 1)
                    n[0] += 1

                def settle():
                    dve.wait_ge(chain1, i * CH + n[0])

                after(dve, chain1, i * CH)
                if now[0]:
                    dve.wait_ge(stats1, Q * (i + 1))
                if now[2]:
                    dve.wait_ge(o_taken, 2 * (i - 1))
                var, u, d2, sm, m2 = tmp
                small_step(V.tensor_tensor(d2[:, 0:Q], st[:, :, 1], st[:, :, 4], ALU.subtract))
                small_step(V.tensor_tensor(sm[:, 0:Q], st[:, :, 1], st[:, :, 4], ALU.add))
                small_step(V.tensor_tensor(m2[:, 0:Q], st[:, :, 2], st[:, :, 5], ALU.add))
                small_step(V.tensor_reduce(var[:, Q:2 * Q], o_sq[s], AX, ALU.add))
                settle()
                small_step(V.scalar_tensor_tensor(d2[:, 0:Q], d2[:, 0:Q], P / 4.0, d2[:, 0:Q],
                                                  ALU.mult, ALU.mult))
                settle()
                small_step(V.scalar_tensor_tensor(var[:, 0:Q], d2[:, 0:Q], P * EPS1, m2[:, 0:Q],
                                                  ALU.add, ALU.add))
                settle()
                small_step(V.tensor_scalar(var[:, 0:Q], var[:, 0:Q], 1.0 / P, None, ALU.mult))
                small_step(V.tensor_scalar(var[:, Q:2 * Q], var[:, Q:2 * Q], 1.0 / D, EPS, ALU.mult, ALU.add))
                settle()
                small_step(V.tensor_scalar(rstd.bitcast(I32), var.bitcast(I32), -0.5, MAGIC, ALU.mult, ALU.add))
                for _ in range(3):
                    settle()
                    small_step(V.scalar_tensor_tensor(u, rstd, -0.5, rstd, ALU.mult, ALU.mult))
                    settle()
                    small_step(V.tensor_tensor(u, u, var, ALU.mult))
                    settle()
                    small_step(V.scalar_tensor_tensor(rstd, u, 1.5, rstd, ALU.add, ALU.mult))
                settle()
                small_step(V.scalar_tensor_tensor(shift, sm[:, 0:Q], -0.5, rstd[:, 0:Q], ALU.mult, ALU.mult))
                assert n[0] == CH

                def add(t):
                    if now[3]:
                        dve.wait_ge(sums1, 2 * (i - 3) + t // 2 + 1)
                        add_tile(added1, i - 3, t, acc[:, :, bass.ds(regs[t], WIN)],
                                 psum[:, 7, (t % 2) * 2 * WIN:(t % 2 + 1) * 2 * WIN].rearrange(
                                     "p (j w) -> p j w", j=2))
                if now[2]:
                    c = C2 * (i - 2)
                    after(dve, sums1, 2 * (i - 3))
                    after(dve, chain2, c)
                    one_hot(onehot[s], i - 2).then_inc(chain2, 1)
                    V.tensor_tensor(y, o_sb[s], rstd[:, Q:2 * Q].unsqueeze(2).to_broadcast([P, Q, D]),
                                    ALU.mult).then_inc(chain2, 1)
                    add(0)
                    dve.wait_ge(chain2, c + 2)
                    y4 = y.rearrange("p (t h) d -> p t (h d)", t=G)
                    V.tensor_tensor(y4, y4, mg[:, :].unsqueeze(1).to_broadcast([P, G, H * D]),
                                    ALU.mult).then_inc(chain2, 1)
                    add(1)
                    dve.wait_ge(chain2, c + 3)
                    V.tensor_tensor(y4, y4, mb[:, :].unsqueeze(1).to_broadcast([P, G, H * D]),
                                    ALU.add).then_inc(chain2, 1)
                    add(2)
                    dve.wait_ge(chain2, c + 4)
                    V.scalar_tensor_tensor(msg[s], y, 0.01, y, ALU.mult, ALU.max).then_inc(chain2, 1)
                    add(3)
                else:
                    for t in range(G):
                        add(t)
            steps(dve, sweep1, NG, 4, 3, u=2)
            dve.wait_ge(added1, T)

            act_done(f"fm{NBLK - 1}")
            scale, shift_ = bn_vectors("bn1", vecs[:, 4:5], vecs[:, 5:6], fm)
            link(V.tensor_scalar(fm, fm, scale, shift_, ALU.mult, ALU.add))
            link(V.scalar_tensor_tensor(fm, fm, 0.01, fm, ALU.mult, ALU.max), mark="y1_f")
            evict("y1_n", lambda c, ps: V.tensor_tensor(xa[:, c, :], spaced(ps, D), xn[:, c, :], ALU.add))
            link(V.tensor_tensor(xa, xa, xn[:, :, :], ALU.add))
            rows_norm(xn[:, :, :], xa, xb, "ln1")

            evict("x2_f", lambda c, ps: V.tensor_copy(fm_c[:, c, :], spaced(ps[0:D], P)))
            evict("table2", lambda c, ps: V.tensor_tensor(
                xa[:, c, :], ps[:, 0:BC * D].rearrange("p (c d) -> p c d", c=BC),
                b2[:, :].unsqueeze(1).to_broadcast([P, BC, D]), ALU.add))
            link(V.tensor_scalar(xa, xa, 0.0, None, ALU.max), mark="t2")
            link(V.memset(acc[:, 0, :], 0.0))
            dve.wait_ge(t2_out, 16)
            plain(p2)
            evict("y2_n", lambda c, ps: V.tensor_tensor(xa[:, c, :], spaced(ps, D), xn[:, c, :], ALU.add))
            rows_norm(xn[:, :, :], xa, xb, "ln2")

            link(V.tensor_tensor(xb, xn[:, :, :], xn[:, :, :], ALU.mult))
            link(V.tensor_reduce(small[:, 0:NC], xb, AX, ALU.add), mark="nrm")
            act_done("nrm")
            link(V.tensor_scalar(small[:, 0:NC], small[:, 0:NC], EPS_NORM, None, ALU.max))
            link(V.reciprocal(dn[:, :], small[:, 0:NC]))
            link(V.tensor_tensor(xa, xn[:, :, :], wide(dn[:, :]), ALU.mult), mark="nh")
            link(V.tensor_copy(tab3[:, :, 0:D], xn[:, :, :]))
            link(V.memset(tab3[:, :, D:SUM3], 1.0))
            link(V.tensor_copy(tab3[:, :, SUM3:ROW3], dn[:, :].unsqueeze(2)), mark="t3")
            link(V.memset(acc[:, 0, :], 0.0))
            link(V.memset(acc[0:D, 1, NP:NW], 0.0))
            evict("nh_f", lambda c, ps: V.tensor_copy(nh_c[:, c, :], spaced(ps[0:D], P)))
            dve.wait_ge(t3_out, 16)
            link(V.memset(pen[:, 0:1], -BIG))
            link(V.memset(pen[:, T:T + 1], -BIG), mark="sweep3")

            def score_step(g, k, s, inside):
                z = s % 2
                one_hot(onehot[z], g).then_inc(a_hot, 1)
                dve.wait_ge(a_hot, g + 1)
                dve.wait_ge(a_dots, g + 1)
                V.tensor_tensor(picked[z], psum[:, 2 + z, :].rearrange("p (t w) -> p t w", t=G), onehot[z],
                                ALU.mult).then_inc(a_pick, 1)
                if inside or g >= 1:
                    after(dve, a_red, g)
                    scale_score(g - 1, (s - 1) % U)
                dve.wait_ge(a_pick, g + 1)
                after(dve, a_score, g - 1)
                V.tensor_reduce(e_raw[z], picked[z], AX, ALU.add).then_inc(a_red, 1)

            def scale_score(g, s):
                V.tensor_tensor(score[:, bass.ds(g * G, G)].unsqueeze(2), e_raw[s % 2].unsqueeze(2),
                                rows3[s][:, :, SUM3:ROW3], ALU.mult).then_inc(a_score, 1)
            steps(dve, score_step, NG, U)
            dve.wait_ge(a_red, NG)
            scale_score(NG - 1, U - 1)
            dve.wait_ge(a_score, NG)
            link(V.tensor_scalar(score, score, beta3[:, 0:1], None, ALU.mult), mark="scores")

            for c, n in enumerate(TC):
                dve.wait_ge(pe_batch, pe_number["turn_out", c])
                link(V.tensor_copy(turned[0:n, c, :], psum[0:n, 4 + c % 4, 0:P]), mark=f"turn_out{c}")
            dve.wait_ge(score_in, 32)
            link(V.tensor_copy(dst_lf, dst_lin))
            link(V.tensor_tensor(pen[:, 1:T], dst_lf[:, 1:T], dst_lf[:, 0:T - 1], ALU.is_equal))
            link(V.tensor_scalar(pen[:, 1:T], pen[:, 1:T], 1.0, BIG, ALU.subtract, ALU.mult))
            link(V.tensor_tensor_scan(fwd, pen[:, 0:T], lin, -BIG, ALU.add, ALU.max))
            link(V.tensor_tensor_scan(seg[:, ::-1], pen[:, 1:T + 1][:, ::-1], fwd[:, ::-1], -BIG, ALU.add, ALU.max))
            for i, at_ in enumerate((0, T - 1)):
                link(V.tensor_copy(ends[:, i:i + 1], dst_lf[:, at_:at_ + 1]))
                link(V.tensor_copy(ends[:, 2 + i:3 + i], seg[:, at_:at_ + 1]), mark="ends")
            dve.wait_ge(ends_in, 32)
            for i in range(2):
                link(V.tensor_scalar(scr_b, ids_b, ends[:, i:i + 1], 1.0, ALU.is_equal, ALU.subtract))
                link(V.scalar_tensor_tensor(scr_b, scr_b, BIG, max_b, ALU.mult, ALU.add))
                link(V.tensor_reduce(ends[:, 4 + i:5 + i], scr_b, AX, ALU.max))
                link(V.tensor_scalar(eq, dst_lf, ends[:, i:i + 1], 1.0, ALU.is_equal, ALU.subtract))
                link(V.tensor_scalar(eq, eq, BIG, ends[:, 4 + i:5 + i], ALU.mult, ALU.add))
                link(V.tensor_tensor(seg, seg, eq, ALU.max), mark="seg")
            for c, n in enumerate(TC):
                dve.wait_ge(pe_batch, pe_number["turn_in", c])
                link(V.tensor_tensor(score[:, c * P:c * P + n], score[:, c * P:c * P + n],
                                     psum[:, 4 + c % 4, 0:n], ALU.subtract), mark=f"turn_in{c}")
            act_done("exp")

            def add3(g, s):
                regs = tile_bases(DVE, g)
                dve.wait_ge(b_sums, g + 1)
                for t in range(G):
                    add_tile(b_added, g, t, acc[0:SUM3, 0, bass.ds(regs[t], WIN)],
                             psum[0:SUM3, s, t * WIN:(t + 1) * WIN])

            def weigh(g, k, s, inside):
                after(dve, b_sums, g - 1)
                for t in range(G):
                    V.tensor_scalar(onehot[s % 2][:, t, :], iota_f[:, :], rel[:, bass.ds(g * G + t, 1)],
                                    score[:, bass.ds(g * G + t, 1)], ALU.is_equal, ALU.mult).then_inc(b_hot, 1)
                if inside or g >= 1:
                    add3(g - 1, (s + 1) % 2)
            steps(dve, weigh, NG, U)
            add3(NG - 1, 1)
            dve.wait_ge(b_added, T)

            for b in range(NB):
                dve.wait_ge(pe_batch, pe_number["y3_n", b])
                c, ps = slice(b * BC, (b + 1) * BC), spaced(node_ps[b % 2], SUM3)
                link(V.tensor_scalar(small[:, 0:BC].unsqueeze(2), ps[:, :, D:SUM3], EPS_NORM, None, ALU.max))
                link(V.reciprocal(small[:, 8:8 + BC], small[:, 0:BC]))
                link(V.tensor_tensor(xa[:, c, :], ps[:, :, 0:D],
                                     small[:, 8:8 + BC].unsqueeze(2).to_broadcast([P, BC, D]), ALU.mult),
                     mark=f"y3_n{b}")
            link(V.tensor_tensor(xa, xa, xn[:, :, :], ALU.add))
            rows_norm(xn[:, :, :], xa, xb, "ln3")

        @block.scalar
        def _(act):
            A = nc.scalar

            def dve_done(mark):
                act.wait_ge(dve_step, marks[mark])

            def root(mark, v):
                dve_done(mark)
                A.activation(v, v, ACT.Sqrt).then_inc(act_step, 1)

            root("deg", hist_sb[:, 0, :])
            root("bn0", small[0:D, 51:52])
            dve_done("bn0_vec")
            A.activation(fm, fm, ACT.Relu, bias=small[0:D, 56:57], scale=small[0:D, 54:55]).then_inc(act_step, 1)
            root("ln0", small[:, 0:NC])

            dve_done("sweep1")

            def sweep1(i, k, s, inside):
                if inside or i < NG:
                    act.wait_ge(xt_turned, i + 1)
                    after(act, m_done, H * (i - 1))
                    A.activation(xt[s][0:D].rearrange("p t n -> p (t n)"), psum[0:D, 0, :],
                                 ACT.Copy).then_inc(xt_ready, 1)
                if inside or i >= 1:
                    z = 1 - s
                    after(act, chain2, C2 * (i - 2))
                    for j in range(2):
                        act.wait_ge(o_done, 2 * (i - 1) + j + 1)
                        pair = slice(2 * j * H, 2 * (j + 1) * H)
                        ps = psum[:, 6, :].rearrange("p (q d) -> p q d", d=D)
                        A.activation(o_sq[z][:, pair, :], ps, ACT.Square)
                        A.activation(o_sb[z][:, pair, :], ps, ACT.Copy).then_inc(o_taken, 1)
                if inside or i < NG:
                    act.wait_ge(chain1, CH * (i + 1))

                    def norm(h):
                        for t in range(G):
                            at_ = alpha[s][:, t, h, :, :].rearrange("p a d -> p (a d)")
                            n = t * H + h
                            A.activation(at_, at_, ACT.Identity, bias=shift[:, n:n + 1],
                                         scale=rstd[:, n:n + 1]).then_inc(normed, 1)

                    def sigmoid(h):
                        act.wait_ge(alpha_t, H * i + h + 1)
                        A.activation(gate[s][:, h, :], psum[:, 2 + h % 2, :], ACT.Sigmoid,
                                     bias=cols[:, 2, h:h + 1], scale=cols[:, 1, h:h + 1]).then_inc(gated, 1)
                    norm(0)
                    for h in range(1, H):
                        norm(h)
                        sigmoid(h - 1)
                    sigmoid(H - 1)
            steps(act, sweep1, NG, 4, 1, u=2)

            for i in range(NBLK):
                act.wait_ge(pe_batch, pe_number["wc", i])
                n = min(512, NP - 512 * i)
                A.activation(fm[:, 512 * i:512 * i + n], psum[0:D, i % 4, 0:n], ACT.Identity,
                             bias=vecs[:, 3:4]).then_inc(act_step, 1)
            root("bn1", small[0:D, 51:52])
            root("ln1", small[:, 0:NC])
            root("ln2", small[:, 0:NC])
            root("nrm", small[:, 0:NC])

            dve_done("sweep3")

            def turned_out(g, k, s, inside):
                act.wait_ge(a_turned, g + 1)
                after(act, a_dots, g - 1)
                A.activation(xs_t[s % 2].rearrange("p t n -> p (t n)"), psum[0:D, 0, :], ACT.Copy).then_inc(a_xt, 1)
            steps(act, turned_out, NG, U)
            dve_done(f"turn_in{len(TC) - 1}")
            A.activation(score, score, ACT.Exp).then_inc(act_step, 1)
            root("ln3", small[:, 0:NC])

        @block.tensor
        def _(pe):
            M = nc.tensor

            def dve_done(mark):
                pe.wait_ge(dve_step, marks[mark])

            def node_pass(name, op):
                for b in range(NB):
                    if b >= 2:
                        dve_done(f"{name}{b - 2}")
                    for j in range(BC):
                        last = op(b * BC + j, node_ps[b % 2], j)
                    last.then_inc(pe_batch, 1)

            def to_nodes(src, n):
                return lambda c, ps, j: M.transpose(ps[:, j * P:j * P + n], src[0:n, c, :], ident[0:n, 0:n])

            def to_features(src):
                return lambda c, ps, j: M.transpose(ps[0:D, j * P:(j + 1) * P], src[:, c, :], ident[:, :])

            def times(w, n):
                return lambda c, ps, j: M.matmul(ps[:, j * n:(j + 1) * n], fm_c[:, c, :], w, start=True, stop=True)

            def hist(g, k, s, inside):
                pe.wait_ge(hot_ready, 2 * (g + 1))
                for t in range(HG):
                    last = M.matmul(psum[0:HI, 0, 0:LO], one_hi[s][:, t, :], one_lo[s][:, t, :],
                                    start=not inside and g == 0 and t == 0,
                                    stop=t == HG - 1, skip_group_check=True)
                last.then_inc(hist_done, 1)
            steps(pe, hist, T // HG, 2, u=2)

            pe.wait_ge(s_load, ALL_IN)
            pe.wait_ge(s_vload, 32)
            for h in range(H):
                last = M.matmul(psum[:, 1, h * P:(h + 1) * P], v_blocks[:, h, :], wu[:, h, :], start=True, stop=True)
            last.then_inc(pe_batch, 1)

            dve_done("fused")
            pe.wait_ge(dinv_in, 16 * 3)
            node_pass("table0", times(w0[:, :], D))
            dve_done(f"table0{NB - 1}")
            for i in range(NBLK):
                n = min(512, NP - 512 * i)
                if i >= 4:
                    dve_done(f"self0{i - 4}")
                M.matmul(psum[0:D, i % 4, 0:n], w0[:, :], fm[:, 512 * i:512 * i + n], start=True, stop=True
                         ).then_inc(pe_batch, 1)

            def plain(p):
                def body(g, k, s, inside):
                    z = s % 2
                    pe.wait_ge(p.rows_in[s], 64 * (k + 1))
                    pe.wait_ge(p.hot, g + 1)
                    after(pe, p.added, G * (g - 1))
                    for t in range(G):
                        last = M.matmul(psum[0:D, z, t * WIN:(t + 1) * WIN], rows[s][:, t, :], onehot[z][:, t, :],
                                        start=True, stop=True)
                    last.then_inc(p.sums, 1)
                steps(pe, body, NG, U)
            dve_done("t0")
            plain(p0)
            pe.wait_ge(act_step, act_number["relu0"])
            node_pass("y0_n", to_nodes(fm_c, D))
            dve_done("ln0_out")
            node_pass("x1_f", to_features(xn[:, :, :]))
            dve_done(f"x1_f{NB - 1}")
            node_pass("table1", times(kv[:, :], H * D))

            dve_done("sweep1")
            pe.wait_ge(bm_in, 48)

            def edge_k(i, k, s, j):
                pe.wait_ge(ea_in[s], 16 * (k + 1))
                after(pe, alpha_e, 2 * i + j)
                for t in range(2):
                    last = M.matmul(psum[:, 1, t * H * D:(t + 1) * H * D], xt[s][D:P, 2 * j + t, :], ke[D:P, :],
                                    start=True, stop=True)
                last.then_inc(ke_done, 1)

            def sweep1(i, k, s, inside):
                now = [inside or 0 <= i - lag < NG for lag in range(4)]
                z = 1 - s

                def m_u(h):
                    after(pe, gm_ready, H * (i - 1) + h - 1)
                    M.matmul(psum[:, 4 + h % 2, :], wvu[:, h, :], xt[z].rearrange("p t n -> p (t n)"),
                             start=True, stop=True).then_inc(m_done, 1)

                def sums(j):
                    after(pe, added1, G * (i - 3) + 2 * j)
                    for t in (2 * j, 2 * j + 1):
                        for half in range(2):
                            at_ = (t % 2 * 2 + half) * WIN
                            last = M.matmul(psum[:, 7, at_:at_ + WIN],
                                            msg[z][:, t * H + 2 * half:t * H + 2 * half + 2, :].rearrange("p h d -> p (h d)"),
                                            onehot[z][:, t, :], start=True, stop=True)
                    last.then_inc(sums1, 1)

                if now[0]:
                    edge_k(i, k, s, 0)
                    pe.wait_ge(kv_in[s], 64 * (k + 1))
                    after(pe, xt_ready, i)
                    pe.sem_inc(turn_go, 1)
                    for t in range(G):
                        last = M.transpose(psum[0:D, 0, t * P:(t + 1) * P], xk[s][:, t, 0:D], ident[:, :])
                    last.then_inc(xt_turned, 1)
                    edge_k(i, k, s, 1)
                if now[1]:
                    pe.wait_ge(xt_ready, i)
                    m_u(0)
                    m_u(1)
                if now[3]:
                    pe.wait_ge(chain2, C2 * (i - 2))
                    sums(0)
                if now[1]:
                    m_u(2)
                    m_u(3)
                    pe.wait_ge(gm_ready, H * i)
                    for j in range(2):
                        after(pe, o_taken, 2 * (i - 1) + j)
                        for t in range(2):
                            at_ = t * H * D
                            for h in range(H):
                                M.matmul(psum[:, 6, at_ + h * D:at_ + (h + 1) * D], gm[:, h, 2 * j + t, :],
                                         wm[:, h, :], start=h == 0, stop=False)
                            last = M.matmul(psum[:, 6, at_:at_ + H * D], ones3[:, :], bm_parts[:, :],
                                            start=False, stop=True)
                        last.then_inc(o_done, 1)

                def turn(h):
                    pe.wait_ge(normed, G * (H * i + h + 1))
                    after(pe, gated, H * i + h - 1)
                    for t in range(G):
                        last = M.transpose(psum[:, 2 + h % 2, t * P:(t + 1) * P],
                                           alpha[s][:, t, h, :, :].rearrange("p a d -> p (a d)"), ident[:, :])
                    last.then_inc(alpha_t, 1)
                if now[0]:
                    turn(0)
                if now[3]:
                    sums(1)
                if now[0]:
                    for h in range(1, H):
                        turn(h)
            steps(pe, sweep1, NG, 4, 3, u=2)

            pe.wait_ge(added1, T)
            for i in range(NBLK):
                n = min(512, NP - 512 * i)
                if i >= 4:
                    pe.wait_ge(act_step, act_number[f"fm{i - 4}"])
                for j in range(2):
                    last = M.matmul(psum[0:D, i % 4, 0:n], wc[:, j, :], acc[:, j, 512 * i:512 * i + n],
                                    start=j == 0, stop=j == 1)
                last.then_inc(pe_batch, 1)
            dve_done("y1_f")
            node_pass("y1_n", to_nodes(fm_c, D))
            dve_done("ln1_out")
            node_pass("x2_f", to_features(xn[:, :, :]))
            dve_done(f"x2_f{NB - 1}")
            node_pass("table2", times(w2[:, :], D))
            dve_done("t2")
            plain(p2)
            pe.wait_ge(p2.added, T)
            node_pass("y2_n", to_nodes(acc_c, D))
            dve_done("nh")
            node_pass("nh_f", to_features(xa))
            dve_done("sweep3")

            def turn3(g, k, s):
                pe.wait_ge(a_in[s], 64 * (k + 1))
                after(pe, a_xt, g)
                pe.sem_inc(turn_go, 1)
                for t in range(G):
                    last = M.transpose(psum[0:D, 0, t * P:(t + 1) * P], rows3[s][:, t, 0:D], ident[:, :])
                last.then_inc(a_turned, 1)

            def dots3(g, s):
                regs = tile_bases(PE, g)
                pe.wait_ge(a_xt, g + 1)
                after(pe, a_pick, g - 1)
                for t in range(G):
                    last = M.matmul(psum[:, 2 + s, t * WIN:(t + 1) * WIN], xs_t[s][:, t, :],
                                    nh_t[:, bass.ds(regs[t], WIN)], start=True, stop=True)
                last.then_inc(a_dots, 1)

            def score_step(g, k, s, inside):
                turn3(g, k, s)
                if inside or g >= 1:
                    dots3(g - 1, (s + 1) % 2)
            steps(pe, score_step, NG, U)
            dots3(NG - 1, 1)

            dve_done("scores")
            for c, n in enumerate(TC):
                if c >= 4:
                    dve_done(f"turn_out{c - 4}")
                M.transpose(psum[0:n, 4 + c % 4, 0:P], score[:, c * P:c * P + n], ident[:, :]).then_inc(pe_batch, 1)
            pe.wait_ge(shift_in, 32)
            for c, n in enumerate(TC):
                if c >= 4:
                    dve_done(f"turn_in{c - 4}")
                M.transpose(psum[:, 4 + c % 4, 0:n], turned[0:n, c, :], ident[0:n, 0:n]).then_inc(pe_batch, 1)

            def weigh(g, k, s, inside):
                pe.wait_ge(b_in[s], 16 * (k + 1))
                pe.wait_ge(b_hot, G * (g + 1))
                after(pe, b_added, G * (g - 1))
                for t in range(G):
                    last = M.matmul(psum[0:SUM3, s % 2, t * WIN:(t + 1) * WIN], rows3[s][:, t, 0:SUM3],
                                    onehot[s % 2][:, t, :],
                                    start=True, stop=True)
                last.then_inc(b_sums, 1)
            steps(pe, weigh, NG, U)
            pe.wait_ge(b_added, T)
            node_pass("y3_n", to_nodes(acc_c, SUM3))

        @block.gpsimd
        def _(pool):
            K = nc.gpsimd
            K.iota(iota_i[:, :], [[1, P]], base=0, channel_multiplier=0).then_inc(s_iota, 1)
            K.iota(part_i[:, :], [[1, 1]], base=0, channel_multiplier=1).then_inc(s_iota, 1)
            pool.wait_ge(s_load, ALL_IN)

            def gather(dst, table, idx, landed):
                pool.sem_inc(gather_go, 1)
                for t in range(G):
                    K.indirect_dma_start(out=dst[:, t, :], out_offset=None, in_=table,
                                         in_offset=bass.IndirectOffsetOnAxis(ap=idx[:, t:t + 1], axis=0)
                                         ).then_inc(landed, 16)

            def plain(p, table):
                def body(g, k, s, inside):
                    after(pool, p.rows_in[s], 64 * k)
                    K.tensor_copy(idx_src[s][:, :], src_t[:, bass.ds(g * G, G)]).then_inc(p.idx, 1)
                    pool.wait_ge(p.idx, g + 1)
                    after(pool, p.sums, g - U + 1)
                    gather(rows[s], table, idx_src[s], p.rows_in[s])
                steps(pool, body, NG, U)
            pool.wait_ge(dve_step, marks["t0"])
            pool.wait_ge(t0_out, 16)
            plain(p0, table0)

            pool.wait_ge(dve_step, marks["sweep1"])

            def sweep1(g, k, s, inside):
                after(pool, kv_in[s], 64 * k)
                after(pool, q_in[s], 64 * k)
                K.tensor_copy(idx_src[s][:, :], src_t[:, bass.ds(g * G, G)]).then_inc(idx_ready, 1)
                K.tensor_copy(idx_dst[s][:, :], dst_t[:, bass.ds(g * G, G)]).then_inc(idx_ready, 1)
                pool.wait_ge(idx_ready, 2 * (g + 1))
                after(pool, alpha_e, 2 * (g - 1))
                after(pool, xt_turned, g - 1)
                gather(xk[s], table1, idx_src[s], kv_in[s])
                gather(q[s].rearrange("p t h d -> p t (h d)"), table1q, idx_dst[s], q_in[s])
            steps(pool, sweep1, NG, 2, u=2)

            pool.wait_ge(dve_step, marks["t2"])
            pool.wait_ge(t2_out, 16)
            plain(p2, table2)

            pool.wait_ge(dve_step, marks["sweep3"])

            def sweep3(g, k, s, inside):
                after(pool, a_in[s], 64 * k)
                K.tensor_copy(idx_src[s][:, :], src_t[:, bass.ds(g * G, G)]).then_inc(a_idx, 1)
                pool.wait_ge(a_idx, g + 1)
                after(pool, a_kept[s], 16 * k)
                after(pool, a_turned, g - U + 1)
                after(pool, a_score, g - U + 1)
                gather(rows3[s], table3, idx_src[s], a_in[s])
            steps(pool, sweep3, NG, U)

        @block.sync
        def _(sp):
            def dve_done(mark):
                sp.wait_ge(dve_step, marks[mark])

            for dst, src in loads:
                sp.dma_start(dst, src).then_inc(s_load, 16)
            dve_done("v_zero")
            sp.dma_start(v_blocks[0:D, :, 0:D], a["vv_t"]).then_inc(s_vload, 16)
            sp.dma_start(v_blocks[D:P, :, D:P], a["ve_t"]).then_inc(s_vload, 16)

            dve_done("dinv")
            sp.dma_start(dinv_flat.rearrange("(h l) -> h l", l=LO), hist_sb[:, 1, :]).then_inc(dinv_out, 16)
            sp.wait_ge(dinv_out, 16)
            sp.dma_start(dn[:, :], dinv_flat.rearrange("(p c) -> p c", c=NC)).then_inc(dinv_in, 16)
            sp.dma_start(dinv_cols, dinv_flat.rearrange("(o n) -> o n", o=1).to_broadcast([D, NP])
                         ).then_inc(dinv_in, 16)
            sp.dma_start(fm, a["x_t"]).then_inc(dinv_in, 16)
            dve_done("bm_parts")
            for i in range(3):
                sp.dma_start(bm_parts[i:i + 1, :], bm_part[i][:, :]).then_inc(bm_in, 16)

            dve_done("t0")
            sp.dma_start(table0.rearrange("(p c) d -> p c d", c=NC), xa).then_inc(t0_out, 16)
            for b in range(NB):
                dve_done(f"table1{b}")
                c = slice(b * BC, (b + 1) * BC)
                sp.dma_start(table1.rearrange("(p c) d -> p c d", c=NC)[:, c, :],
                             stage[b % 2]).then_inc(t1_out[b % 2], 16)
                sp.dma_start(table1q.rearrange("(p c) d -> p c d", c=NC)[:, c, :],
                             stage[b % 2][:, :, D:ROW1]).then_inc(t1_out[b % 2], 16)

            dve_done("sweep1")

            def edges(g, k, s, inside):
                after(sp, m_done, H * (g - 1))
                sp.dma_start(xt[s][D:P].rearrange("p t n -> p (t n)"),
                             a["edge_t"][:, bass.ds(g * G * P, G * P)]).then_inc(ea_in[s], 16)
            steps(sp, edges, NG, 2, u=2)

            dve_done("t2")
            sp.dma_start(table2.rearrange("(p c) d -> p c d", c=NC), xa).then_inc(t2_out, 16)
            dve_done("t3")
            sp.dma_start(table3.rearrange("(p c) d -> p c d", c=NC), tab3).then_inc(t3_out, 16)

            def keep(g, k, s, inside):
                sp.wait_ge(a_in[s], 64 * (k + 1))
                sp.dma_start(kept_rows[g, :, :] if not inside else kept_rows[bass.ds(g, 1), :, :].rearrange("o p n -> (o p) n"),
                             rows3[s].rearrange("p t n -> p (t n)")).then_inc(a_kept[s], 16)
            steps(sp, keep, NG, U)

            dve_done(f"turn_out{len(TC) - 1}")
            full = (T // P) * P * P

            def turned_dma(flat, out_, landed):
                pairs = [(flat[0:full].rearrange("(c t e) -> t c e", t=P, e=P), turned[:, 0:T // P, :]),
                         (flat[full:T * P].rearrange("(t e) -> t e", e=P), turned[0:TC[-1], T // P, :])]
                for d, s_ in pairs:
                    sp.dma_start(*((d, s_) if out_ else (s_, d))).then_inc(landed, 16)
            turned_dma(score_lin, True, score_out)
            sp.wait_ge(score_out, 32)
            sp.dma_start(lin, score_lin.rearrange("(p j) -> p j", p=P)).then_inc(score_in, 16)
            sp.dma_start(dst_lin, a["dst_l"]).then_inc(score_in, 16)
            dve_done("ends")
            sp.dma_start(edge_ids.rearrange("(p i) -> p i", i=2), ends[:, 0:2]).then_inc(ends_out, 16)
            sp.dma_start(edge_max.rearrange("(p i) -> p i", i=2), ends[:, 2:4]).then_inc(ends_out, 16)
            sp.wait_ge(ends_out, 32)
            for dst, src in ((ids_b, edge_ids), (max_b, edge_max)):
                sp.dma_start(dst, src.rearrange("(o n) -> o n", o=1).to_broadcast([P, 2 * P])).then_inc(ends_in, 16)
            dve_done("seg")
            sp.dma_start(shift_lin.rearrange("(p j) -> p j", p=P), seg).then_inc(shift_out, 16)
            sp.wait_ge(shift_out, 16)
            turned_dma(shift_lin, False, shift_in)

            for s in range(U):
                sp.wait_ge(a_kept[s], 16 * (NG // U))

            def fetch(g, k, s, inside):
                after(sp, b_sums, g - U + 1)
                sp.dma_start(rows3[s].rearrange("p t n -> p (t n)"),
                             kept_rows[g, :, :] if not inside else kept_rows[bass.ds(g, 1), :, :].rearrange("o p n -> (o p) n")
                             ).then_inc(b_in[s], 16)
            steps(sp, fetch, NG, U)

            dve_done("ln3_out")
            whole = N // NC
            sp.dma_start(out[0:whole * NC, :].rearrange("(p c) d -> p c d", c=NC), xn[0:whole, :, :]).then_inc(out_done, 16)
            sp.dma_start(out[whole * NC:N, :].rearrange("(o c) d -> o c d", o=1), xn[whole:whole + 1, 0:N - whole * NC, :]
                         ).then_inc(out_done, 16)
            sp.wait_ge(out_done, 32)


def kernel(**inputs):
    import numpy as np
    import concourse.bacc as bacc
    from concourse.bass_utils import run_bass_kernel_spmd

    x, src, dst = (np.asarray(inputs[n]) for n in ("x", "src", "dst"))
    edges = np.asarray(inputs["edge_attr_64"])

    def get(name):
        return np.asarray(inputs[name])

    def c(v):
        return np.ascontiguousarray(v)

    pad = T * P - E
    dst_p = np.concatenate([dst, np.full(pad, N, dst.dtype)])
    src_p = np.concatenate([src, np.zeros(pad, src.dtype)])
    x_p = np.concatenate([x, np.zeros((NP - N, D), x.dtype)])
    edge_t = np.zeros((D, T * P), edges.dtype)
    edge_t[:, :E] = edges.T
    arrays = {
        "src_t": c(src_p.reshape(T, P).T), "dst_t": c(dst_p.reshape(T, P).T), "dst_l": c(dst_p.reshape(P, T)),
        "x": x_p, "x_t": c(x_p.T), "edge_t": edge_t,
        "w0": get("L0_gnn_W"), "w2": get("L2_gnn_W"),
        "kv": c(get("L1_gnn_Kv2v").transpose(1, 0, 2).reshape(D, H * D)),
        "ke": c(get("L1_gnn_Ke2v").transpose(1, 0, 2).reshape(D, H * D)),
        "vv_t": c(get("L1_gnn_Vv2v").transpose(2, 0, 1)), "ve_t": c(get("L1_gnn_Ve2v").transpose(2, 0, 1)),
        "wu": c(get("L1_gnn_Wu").transpose(1, 0, 2)), "wm": c(get("L1_gnn_Wm").transpose(1, 0, 2)),
        "wc": c(get("L1_gnn_Wc").reshape(2, P, D).transpose(1, 0, 2)),
        "cols": c(np.stack([get("L1_gnn_" + n).T for n in ("bu", "ln_g", "ln_b")], axis=1)),
        "vecs": c(np.stack([get(n) for n in ("L0_gnn_b", "L0_gnn_gamma", "L0_gnn_beta", "L1_gnn_bc",
                                             "L1_gnn_bn_g", "L1_gnn_bn_b")], axis=1)),
        "bm": get("L1_gnn_bm").reshape(1, H, D),
        "mg": get("L1_gnn_mln_g").reshape(1, H * D), "mb": get("L1_gnn_mln_b").reshape(1, H * D),
        "b2": get("L2_gnn_b").reshape(1, D), "beta3": get("L3_gnn_beta").reshape(1, 1),
    }
    nc = bacc.Bacc("TRN2", target_bir_lowering=False, num_devices=1)
    aps = {n: nc.dram_tensor("in_" + n, v.shape, mybir.dt.from_np(v.dtype), kind="ExternalInput").ap()
           for n, v in arrays.items()}
    out = nc.dram_tensor("out", (N, D), F32, kind="ExternalOutput").ap()
    gnn(nc, aps, out)
    r = run_bass_kernel_spmd(nc, [{"in_" + n: v for n, v in arrays.items()}], core_ids=[0])
    return r.results[0]["out"]
```
